# Optimizing a Trainium2 kernel written in Bass

```python
import numpy as np
import jax
import jax.numpy as jnp

def _softmax(x, axis=-1):
    return jax.nn.softmax(x, axis=axis)

def _gelu(x):
    return jax.nn.gelu(x, approximate=True)

def _silu(x):
    return jax.nn.silu(x)

def _sigmoid(x):
    return jax.nn.sigmoid(x)

def _layernorm(x, axis=-1, eps=1e-05):
    m = jnp.mean(x, axis=axis, keepdims=True)
    v = jnp.var(x, axis=axis, keepdims=True)
    return (x - m) / jnp.sqrt(v + eps)

def _scatter_add(tgt, idx, src, axis=0):
    return tgt.at[idx].add(src)

def _segment_sum(src, seg, n):
    return jax.ops.segment_sum(src, seg, n)
kernel_name = 'mk_dlrm_tower_d1_rec_r8_c60c62'

def setup_inputs(seed: int=0):
    np.random.seed(seed)
    _w = jnp.asarray

    def _rec_inputs():
        import jax
        import jax.numpy as jnp
        _tk = jax.random.key(seed)
        ids = jnp.stack([jax.random.randint(jax.random.fold_in(_tk, 200 + f), (512,), 0, v, jnp.int32) for f, v in enumerate([1250, 1250, 1000, 1000, 1250, 12500, 1250, 1000, 1250, 12500, 1250, 1000, 1250, 12500, 1000, 12500, 12500, 125000, 12500, 1250, 12500, 1250, 1250, 1250, 1000, 1000])], axis=1)
        tbl_0 = 0.05 * jax.random.normal(jax.random.fold_in(_tk, 500 + 0), (1250, 128), jnp.float32)
        tbl_1 = 0.05 * jax.random.normal(jax.random.fold_in(_tk, 500 + 1), (1250, 128), jnp.float32)
        tbl_2 = 0.05 * jax.random.normal(jax.random.fold_in(_tk, 500 + 2), (1000, 128), jnp.float32)
        tbl_3 = 0.05 * jax.random.normal(jax.random.fold_in(_tk, 500 + 3), (1000, 128), jnp.float32)
        tbl_4 = 0.05 * jax.random.normal(jax.random.fold_in(_tk, 500 + 4), (1250, 128), jnp.float32)
        tbl_5 = 0.05 * jax.random.normal(jax.random.fold_in(_tk, 500 + 5), (12500, 128), jnp.float32)
        tbl_6 = 0.05 * jax.random.normal(jax.random.fold_in(_tk, 500 + 6), (1250, 128), jnp.float32)
        tbl_7 = 0.05 * jax.random.normal(jax.random.fold_in(_tk, 500 + 7), (1000, 128), jnp.float32)
        tbl_8 = 0.05 * jax.random.normal(jax.random.fold_in(_tk, 500 + 8), (1250, 128), jnp.float32)
        tbl_9 = 0.05 * jax.random.normal(jax.random.fold_in(_tk, 500 + 9), (12500, 128), jnp.float32)
        tbl_10 = 0.05 * jax.random.normal(jax.random.fold_in(_tk, 500 + 10), (1250, 128), jnp.float32)
        tbl_11 = 0.05 * jax.random.normal(jax.random.fold_in(_tk, 500 + 11), (1000, 128), jnp.float32)
        tbl_12 = 0.05 * jax.random.normal(jax.random.fold_in(_tk, 500 + 12), (1250, 128), jnp.float32)
        tbl_13 = 0.05 * jax.random.normal(jax.random.fold_in(_tk, 500 + 13), (12500, 128), jnp.float32)
        tbl_14 = 0.05 * jax.random.normal(jax.random.fold_in(_tk, 500 + 14), (1000, 128), jnp.float32)
        tbl_15 = 0.05 * jax.random.normal(jax.random.fold_in(_tk, 500 + 15), (12500, 128), jnp.float32)
        tbl_16 = 0.05 * jax.random.normal(jax.random.fold_in(_tk, 500 + 16), (12500, 128), jnp.float32)
        tbl_17 = 0.05 * jax.random.normal(jax.random.fold_in(_tk, 500 + 17), (125000, 128), jnp.float32)
        tbl_18 = 0.05 * jax.random.normal(jax.random.fold_in(_tk, 500 + 18), (12500, 128), jnp.float32)
        tbl_19 = 0.05 * jax.random.normal(jax.random.fold_in(_tk, 500 + 19), (1250, 128), jnp.float32)
        tbl_20 = 0.05 * jax.random.normal(jax.random.fold_in(_tk, 500 + 20), (12500, 128), jnp.float32)
        tbl_21 = 0.05 * jax.random.normal(jax.random.fold_in(_tk, 500 + 21), (1250, 128), jnp.float32)
        tbl_22 = 0.05 * jax.random.normal(jax.random.fold_in(_tk, 500 + 22), (1250, 128), jnp.float32)
        tbl_23 = 0.05 * jax.random.normal(jax.random.fold_in(_tk, 500 + 23), (1250, 128), jnp.float32)
        tbl_24 = 0.05 * jax.random.normal(jax.random.fold_in(_tk, 500 + 24), (1000, 128), jnp.float32)
        tbl_25 = 0.05 * jax.random.normal(jax.random.fold_in(_tk, 500 + 25), (1000, 128), jnp.float32)
        _rk = jax.random.fold_in(_tk, 7)
        r_dense_features = -0.000520686 + 1.00062 * jax.random.normal(jax.random.fold_in(_rk, 101), (512, 128), jnp.float32)
        W_top1 = 0.0405887 * jax.random.normal(jax.random.fold_in(_tk, 801), (607, 512), jnp.float32)
        W_top2 = 0.0441942 * jax.random.normal(jax.random.fold_in(_tk, 802), (512, 256), jnp.float32)
        W_top3 = 0.0625 * jax.random.normal(jax.random.fold_in(_tk, 803), (256, 1), jnp.float32)
        b_top1 = jnp.zeros((512,), jnp.float32)
        b_top2 = jnp.zeros((256,), jnp.float32)
        return (r_dense_features, ids, tbl_0, tbl_1, tbl_2, tbl_3, tbl_4, tbl_5, tbl_6, tbl_7, tbl_8, tbl_9, tbl_10, tbl_11, tbl_12, tbl_13, tbl_14, tbl_15, tbl_16, tbl_17, tbl_18, tbl_19, tbl_20, tbl_21, tbl_22, tbl_23, tbl_24, tbl_25, W_top1, b_top1, W_top2, b_top2, W_top3)
    r_dense_features, ids, tbl_0, tbl_1, tbl_2, tbl_3, tbl_4, tbl_5, tbl_6, tbl_7, tbl_8, tbl_9, tbl_10, tbl_11, tbl_12, tbl_13, tbl_14, tbl_15, tbl_16, tbl_17, tbl_18, tbl_19, tbl_20, tbl_21, tbl_22, tbl_23, tbl_24, tbl_25, W_top1, b_top1, W_top2, b_top2, W_top3 = _rec_inputs()

    def _L0_rec_setup():
        import jax, jax.numpy as jnp
        import numpy as np
        B, F, D = (2048, 26, 128)
        key = jax.random.key(seed)
        k1, k2 = jax.random.split(key)
        dense_features = jax.random.normal(k1, (B, D), dtype=jnp.float32)
        sparse_values = jax.random.normal(k2, (B, F, D), dtype=jnp.float32)
        return {'dense_features': dense_features, 'sparse_values': sparse_values}
    _L0_rec_all = _L0_rec_setup()
    _L0_rec_in = {k: v for k, v in _L0_rec_all.items() if k in ()}
    del _L0_rec_all
    return {'r_dense_features': r_dense_features, 'ids': ids, 'tbl_0': tbl_0, 'tbl_1': tbl_1, 'tbl_2': tbl_2, 'tbl_3': tbl_3, 'tbl_4': tbl_4, 'tbl_5': tbl_5, 'tbl_6': tbl_6, 'tbl_7': tbl_7, 'tbl_8': tbl_8, 'tbl_9': tbl_9, 'tbl_10': tbl_10, 'tbl_11': tbl_11, 'tbl_12': tbl_12, 'tbl_13': tbl_13, 'tbl_14': tbl_14, 'tbl_15': tbl_15, 'tbl_16': tbl_16, 'tbl_17': tbl_17, 'tbl_18': tbl_18, 'tbl_19': tbl_19, 'tbl_20': tbl_20, 'tbl_21': tbl_21, 'tbl_22': tbl_22, 'tbl_23': tbl_23, 'tbl_24': tbl_24, 'tbl_25': tbl_25, 'W_top1': W_top1, 'b_top1': b_top1, 'W_top2': W_top2, 'b_top2': b_top2, 'W_top3': W_top3}

def reference(r_dense_features, ids, tbl_0, tbl_1, tbl_2, tbl_3, tbl_4, tbl_5, tbl_6, tbl_7, tbl_8, tbl_9, tbl_10, tbl_11, tbl_12, tbl_13, tbl_14, tbl_15, tbl_16, tbl_17, tbl_18, tbl_19, tbl_20, tbl_21, tbl_22, tbl_23, tbl_24, tbl_25, W_top1, b_top1, W_top2, b_top2, W_top3):
    import jax
    import jax.numpy as jnp

    def _L0_rec_ref(dense_features, sparse_values):
        import jax, jax.numpy as jnp
        import numpy as np
        B, F, D = (2048, 26, 128)
        sd = jnp.einsum('bfd,bd->bf', sparse_values, dense_features)
        ss = jnp.einsum('bfd,bgd->bfg', sparse_values, sparse_values)
        iu, ju = jnp.triu_indices(F, k=1)
        pairs = ss[:, iu, ju]
        return jnp.concatenate([dense_features, sd, pairs], axis=1)
    e = jnp.stack([tbl_0[ids[:, 0]], tbl_1[ids[:, 1]], tbl_2[ids[:, 2]], tbl_3[ids[:, 3]], tbl_4[ids[:, 4]], tbl_5[ids[:, 5]], tbl_6[ids[:, 6]], tbl_7[ids[:, 7]], tbl_8[ids[:, 8]], tbl_9[ids[:, 9]], tbl_10[ids[:, 10]], tbl_11[ids[:, 11]], tbl_12[ids[:, 12]], tbl_13[ids[:, 13]], tbl_14[ids[:, 14]], tbl_15[ids[:, 15]], tbl_16[ids[:, 16]], tbl_17[ids[:, 17]], tbl_18[ids[:, 18]], tbl_19[ids[:, 19]], tbl_20[ids[:, 20]], tbl_21[ids[:, 21]], tbl_22[ids[:, 22]], tbl_23[ids[:, 23]], tbl_24[ids[:, 24]], tbl_25[ids[:, 25]]], axis=1)
    z = _L0_rec_ref(r_dense_features, e)
    z = z.reshape(z.shape[0], -1)
    h = jnp.concatenate([z, r_dense_features], axis=1)
    h = jnp.maximum(h @ W_top1 + b_top1, 0.0)
    h = jnp.maximum(h @ W_top2 + b_top2, 0.0)
    y = h @ W_top3
    return y

_drawn_inputs = setup_inputs


def setup_inputs(seed=0):
    import zlib

    import numpy as np

    out = dict(_drawn_inputs(seed))
    spreads = {'b_top1': (0.0, 0.1), 'b_top2': (0.0, 0.1)}
    factors = {}
    for name, (base, spread) in spreads.items():
        noise = np.random.default_rng([zlib.crc32(name.encode()), seed]).standard_normal(out[name].shape)
        drawn = base * np.exp(spread * noise) if base else spread * noise
        out[name] = jnp.asarray(drawn.astype(out[name].dtype))
    for name, factor in factors.items():
        out[name] = (out[name] * factor).astype(out[name].dtype)
    return out
```

```python
def dlrm_tower(nc, r_dense_features, ids, tables, W_top1, b_top1, W_top2, b_top2, W_top3, out):
    import concourse.bass as bass
    from concourse import mybir
    from contextlib import ExitStack

    fp32 = mybir.dt.float32
    i32 = mybir.dt.int32
    ALU = mybir.AluOpType
    ACT = mybir.ActivationFunctionType

    P = 128
    B, F = ids.shape
    D = tables[0].shape[1]
    H1, H2 = W_top2.shape
    NT = B // P
    QUAD = 32
    SPG = P // QUAD
    NV = F + 1
    DENSE = F
    GPT = P // SPG
    GPB = 8
    NG = GPT // GPB
    NC = -(-F // SPG)
    N1 = H1 // P
    N2 = H2 // P
    ONE = NV

    SLOTS = [(24, 3), (20, 4), (16, 4), (12, 4), (8, 4), (4, 4), (0, 4)]
    NQ = len(SLOTS)

    def width(j):
        return len(range(j, F, SPG))

    with ExitStack() as ctx:
        def sb(name, shape, dt=fp32):
            return ctx.enter_context(nc.sbuf_tensor(name, shape, dt))

        def ps(name, shape):
            return ctx.enter_context(nc.psum_tensor(name, shape, fp32))

        def sem(name):
            return ctx.enter_context(nc.semaphore(name))

        ids_sb = sb("ids_sb", [P, NT, F], i32)
        dense = sb("dense", [P, NT, D])
        emb = sb("emb", [P, NT, F, D])
        vecT = sb("vecT", [P, B, QUAD])
        pairs = sb("pairs", [P, NC, B])
        w1_pair = sb("w1_pair", [P, NC, H1])
        w1_dense = sb("w1_dense", [P, 2, H1])
        w1_sum = sb("w1_sum", [P, H1])
        w2 = sb("w2", [P, N1, H2])
        w3 = sb("w3", [P, N2])
        b2 = sb("b2", [P, N2])
        h1T = sb("h1T", [P, N1, B])
        h2T = sb("h2T", [P, N2, B])
        y = sb("y", [1, P, NT])
        ident = sb("ident", [P, P])

        tp = [ps(f"tp{i}", [P, 4, P]) for i in range(2)]
        gram = [ps(f"gram{i}", [P, GPB, P]) for i in range(2)]
        mlp1 = ps("mlp1", [P, N1, P])
        mlp2 = ps("mlp2", [P, 4, P])

        ids_in = sem("ids_in")
        dense_in = sem("dense_in")
        gathered = [[sem(f"gathered{t}_{q}") for q in range(NQ)] for t in range(NT)]
        w1_in = sem("w1_in")
        wd_in = sem("wd_in")
        w23_in = sem("w23_in")
        w1_zero = sem("w1_zero")
        pads_set = sem("pads_set")
        ident_zero = sem("ident_zero")
        ident_set = sem("ident_set")
        wsum_set = sem("wsum_set")
        transposed = sem("transposed")
        vec_set = sem("vec_set")
        gram_done = sem("gram_done")
        pairs_act = sem("pairs_act")
        pairs_dve = sem("pairs_dve")
        mlp1_done = sem("mlp1_done")
        h1_set = sem("h1_set")
        mlp2_done = sem("mlp2_done")
        h2_set = sem("h2_set")
        mlp3_done = sem("mlp3_done")
        y_set = sem("y_set")
        y_out = sem("y_out")

        block = ctx.enter_context(nc.Block())

        @block.sync
        def _(sp):
            sp.dma_start(ids_sb[:], ids.rearrange("(p t) f -> p t f", t=NT)).then_inc(ids_in, 16)
            sp.dma_start(dense[:], r_dense_features.rearrange("(p t) d -> p t d", t=NT)).then_inc(dense_in, 16)
            sp.dma_start(w1_dense[:, 0], W_top1[0:D, :]).then_inc(wd_in, 16)
            sp.dma_start(w1_dense[:, 1], W_top1[W_top1.shape[0] - D:, :]).then_inc(wd_in, 16)
            sp.wait_ge(w1_zero, 1)
            row = D + F
            for i in range(F):
                j, c = i % SPG, i // SPG
                if i < F - 1:
                    n = F - 1 - i
                    sp.dma_start(w1_pair[QUAD * j + i + 1:QUAD * j + F, c, :],
                                 W_top1[row:row + n, :]).then_inc(w1_in, 16)
                    row += n
            for j in range(SPG):
                n = width(j)
                sp.dma_start(w1_pair[QUAD * j + DENSE:QUAD * j + DENSE + 1, 0:n, :],
                             W_top1[D + j:D + j + SPG * (n - 1) + 1:SPG, :].rearrange("(o c) n -> o c n", o=1)
                             ).then_inc(w1_in, 16)
            sp.dma_start(w1_pair[ONE:ONE + 1, 0, :], b_top1.rearrange("(o n) -> o n", o=1)).then_inc(w1_in, 16)
            sp.dma_start(w2[:], W_top2.rearrange("(k p) n -> p k n", p=P)).then_inc(w23_in, 16)
            with nc.allow_non_contiguous_dma(reason="two short columns"):
                sp.dma_start(w3[:], W_top3.rearrange("(k p) o -> p (k o)", p=P)).then_inc(w23_in, 16)
                sp.dma_start(b2[:], b_top2.rearrange("(k p) -> p k", p=P)).then_inc(w23_in, 16)
            sp.wait_ge(y_set, NT)
            sp.dma_start(out.rearrange("(o b) n -> o (b n)", o=1), y[:].rearrange("o p t -> o (p t)")).then_inc(y_out, 16)
            sp.wait_ge(y_out, 16)

        W1_LOADS = (F - 1) + SPG + 1

        @block.gpsimd
        def _(pool):
            nc.gpsimd.memset(ident[:], 0.0).then_inc(ident_zero, 1)
            pool.wait_ge(ident_zero, 1)
            nc.gpsimd.affine_select(out=ident[:], in_=ident[:], compare_op=ALU.not_equal, fill=1.0,
                                    base=0, pattern=[[-1, P]], channel_multiplier=1).then_inc(ident_set, 1)
            pool.wait_ge(ids_in, 16)
            for t in range(NT):
                for q, (s0, n) in enumerate(SLOTS):
                    for f in range(s0, min(s0 + n, F)):
                        nc.gpsimd.indirect_dma_start(emb[:, t, f, :], None, tables[f],
                                                     bass.IndirectOffsetOnAxis(ids_sb[:, t, f:f + 1], 0)
                                                     ).then_inc(gathered[t][q], 16)

        def pair_copy(engine, t, g, s, j):
            n = width(j)
            src = gram[(t * NG + g) % 2][QUAD * s:QUAD * s + NV, :, s * F + j:s * F + j + SPG * (n - 1) + 1:SPG]
            b0 = t * P + g * GPB * SPG + s
            dst = pairs[QUAD * j:QUAD * j + NV, 0:n, b0:b0 + SPG * (GPB - 1) + 1:SPG].rearrange("p c g -> p g c")
            return engine(dst, src)

        @block.scalar
        def _(act):
            def slots_out(t, q):
                s0, n = SLOTS[q]
                act.wait_ge(transposed, t * NQ + q + 1)
                nc.scalar.copy(vecT[:, t * P:(t + 1) * P, s0:s0 + n].rearrange("p b s -> p s b"),
                               tp[(t * NQ + q) % 2][:, 0:n, :]).then_inc(vec_set, 1)

            def pairs_out(t, g):
                act.wait_ge(gram_done, t * NG + g + 1)
                for s in range(2):
                    for j in range(SPG):
                        last = pair_copy(nc.scalar.copy, t, g, s, j)
                last.then_inc(pairs_act, 1)

            def h2_out(t):
                act.wait_ge(mlp2_done, t + 1)
                act.wait_ge(w23_in, 48)
                for k in range(N2):
                    last = nc.scalar.activation(h2T[:, k, t * P:(t + 1) * P], mlp2[:, k, :], ACT.Relu,
                                                bias=b2[:, k:k + 1])
                last.then_inc(h2_set, 1)

            act.wait_ge(pads_set, 2)
            for t in range(NT + 1):
                for q in range(NQ):
                    if t < NT:
                        slots_out(t, q)
                    if t > 0 and q < NG:
                        pairs_out(t - 1, q)
                    if t > 0 and q == NG + 1:
                        h2_out(t - 1)

        @block.vector
        def _(dve):
            nc.vector.memset(w1_pair[:], 0.0).then_inc(w1_zero, 1)
            nc.vector.memset(vecT[:, :, NV:QUAD], 0.0).then_inc(pads_set, 1)
            nc.vector.memset(pairs[:], 1.0).then_inc(pads_set, 1)
            dve.wait_ge(wd_in, 32)
            nc.vector.tensor_tensor(w1_sum[:], w1_dense[:, 0], w1_dense[:, 1], ALU.add).then_inc(wsum_set, 1)
            dve.wait_ge(pads_set, 2)
            for t in range(NT):
                for g in range(NG):
                    dve.wait_ge(gram_done, t * NG + g + 1)
                    for s in range(2, SPG):
                        for j in range(SPG):
                            last = pair_copy(nc.vector.tensor_copy, t, g, s, j)
                    last.then_inc(pairs_dve, 1)
                dve.wait_ge(mlp1_done, t + 1)
                nc.vector.tensor_scalar_max(h1T[:, :, t * P:(t + 1) * P], mlp1[:], 0.0).then_inc(h1_set, 1)
                dve.wait_ge(mlp3_done, t + 1)
                nc.vector.tensor_copy(y[:, :, t], mlp2[0:1, N2, :]).then_inc(y_set, 1)

        @block.tensor
        def _(pe):
            def transposes(t, q):
                s0, n = SLOTS[q]
                k = t * NQ + q
                if k >= 2:
                    pe.wait_ge(vec_set, k - 1)
                pe.wait_ge(gathered[t][q], 16 * (min(s0 + n, F) - s0))
                for s in range(n):
                    src = dense[:, t, :] if s0 + s == DENSE else emb[:, t, s0 + s, :]
                    last = nc.tensor.transpose(tp[k % 2][:, s, :], src, ident[:])
                last.then_inc(transposed, 1)

            def grams(t, g):
                k = t * NG + g
                pe.wait_ge(vec_set, NQ * (t + 1))
                if k >= 2:
                    pe.wait_ge(pairs_act, k - 1)
                    pe.wait_ge(pairs_dve, k - 1)
                for i in range(GPB):
                    b0 = t * P + (g * GPB + i) * SPG
                    last = nc.tensor.matmul(gram[k % 2][:, i, 0:SPG * F],
                                            vecT[:, b0:b0 + SPG, :].rearrange("p b s -> p (b s)"),
                                            vecT[:, b0:b0 + SPG, 0:F], start=True, stop=True)
                last.then_inc(gram_done, 1)

            def layer1(t):
                if t > 0:
                    pe.wait_ge(h1_set, t)
                else:
                    pe.wait_ge(w1_in, 16 * W1_LOADS)
                    pe.wait_ge(wsum_set, 1)
                pe.wait_ge(pairs_act, NG * (t + 1))
                pe.wait_ge(pairs_dve, NG * (t + 1))
                cols = slice(t * P, (t + 1) * P)
                for n in range(N1):
                    ns = slice(n * P, (n + 1) * P)
                    last = nc.tensor.matmul(mlp1[:, n, :], w1_sum[:, ns], vecT[:, cols, DENSE], start=True, stop=False)
                    for c in range(NC):
                        rows = QUAD * min(SPG, F - c * SPG)
                        last = nc.tensor.matmul(mlp1[:, n, :], w1_pair[0:rows, c, ns], pairs[0:rows, c, cols],
                                                start=False, stop=c == NC - 1)
                last.then_inc(mlp1_done, 1)

            def layer23(t):
                cols = slice(t * P, (t + 1) * P)
                pe.wait_ge(h1_set, t + 1)
                if t > 0:
                    pe.wait_ge(y_set, t)
                else:
                    pe.wait_ge(w23_in, 48)
                for n in range(N2):
                    for k in range(N1):
                        last = nc.tensor.matmul(mlp2[:, n, :], w2[:, k, n * P:(n + 1) * P], h1T[:, k, cols],
                                                start=k == 0, stop=k == N1 - 1)
                last.then_inc(mlp2_done, 1)

            def layer3(t):
                cols = slice(t * P, (t + 1) * P)
                pe.wait_ge(h2_set, t + 1)
                for k in range(N2):
                    last = nc.tensor.matmul(mlp2[0:1, N2, :], w3[:, k:k + 1], h2T[:, k, cols],
                                            start=k == 0, stop=k == N2 - 1)
                last.then_inc(mlp3_done, 1)

            pe.wait_ge(ident_set, 1)
            pe.wait_ge(dense_in, 16)
            for t in range(NT + 1):
                for q in range(NQ):
                    if t < NT:
                        transposes(t, q)
                    if t > 0:
                        if q < NG:
                            grams(t - 1, q)
                        elif q == NG:
                            layer1(t - 1)
                        elif q == NG + 1:
                            layer23(t - 1)
                        elif q == NG + 2:
                            layer3(t - 1)


def kernel(**inputs):
    import numpy as np
    import concourse.bacc as bacc
    from concourse import mybir
    from concourse.bass_utils import run_bass_kernel_spmd

    nc = bacc.Bacc("TRN2", target_bir_lowering=False, num_devices=1)
    arrays, aps = {}, {}
    for name, value in inputs.items():
        a = np.ascontiguousarray(value)
        arrays[f"in_{name}"] = a
        aps[name] = nc.dram_tensor(f"in_{name}", a.shape, mybir.dt.from_np(a.dtype), kind="ExternalInput").ap()
    batch, features = inputs["ids"].shape
    out = nc.dram_tensor("out_y", (batch, 1), mybir.dt.float32, kind="ExternalOutput").ap()
    dlrm_tower(nc, aps["r_dense_features"], aps["ids"], [aps[f"tbl_{f}"] for f in range(features)],
               aps["W_top1"], aps["b_top1"], aps["W_top2"], aps["b_top2"], aps["W_top3"], out)
    return run_bass_kernel_spmd(nc, [arrays], core_ids=[0]).results[0]["out_y"]
```

```python
def dlrm_tower(nc, r_dense_features, ids, ids_cols, tables, W_top1, b_top1, W_top2, b_top2, W_top3, out):
    import concourse.bass as bass
    from concourse import mybir
    from contextlib import ExitStack

    fp32 = mybir.dt.float32
    i32 = mybir.dt.int32
    fp16 = mybir.dt.float16
    bf16 = mybir.dt.bfloat16
    ALU = mybir.AluOpType
    ACT = mybir.ActivationFunctionType

    P = 128
    B, F = ids.shape
    D = tables[0].shape[1]
    H1, H2 = W_top2.shape
    NT = B // P
    QUAD = 32
    SPG = P // QUAD
    NV = F + 1
    DENSE = F
    GPT = P // SPG
    GPB = 8
    NG = GPT // GPB
    NC = -(-F // SPG)
    N1 = H1 // P
    N2 = H2 // P
    M = QUAD * (SPG - 1) + NV
    ONE = NV

    HOT = [25, 24, 14, 11]
    HC = 8
    HP = tables[HOT[0]].shape[0] // HC
    assert all(tables[f].shape[0] == HP * HC <= 2048 for f in HOT) and HP <= P
    HS = HP // 16 * 16
    NH = len(HOT)

    SLOTS = [[21, 22, 23, DENSE], [17, 18, 19, 20], [12, 13, 15, 16], [8, 9, 10], [4, 5, 6, 7], [0, 1, 2, 3]]
    NQ = len(SLOTS)
    assert sorted(sum(SLOTS, HOT)) == list(range(NV))

    def runs(q):
        found = []
        for at, slot in enumerate(SLOTS[q]):
            if found and found[-1][1] + found[-1][2] == slot:
                found[-1][2] += 1
            else:
                found.append([at, slot, 1])
        return found

    def width(j):
        return len(range(j, F, SPG))

    with ExitStack() as ctx:
        def sb(name, shape, dt=fp32):
            return ctx.enter_context(nc.sbuf_tensor(name, shape, dt))

        def ps(name, shape):
            return ctx.enter_context(nc.psum_tensor(name, shape, fp32))

        def sem(name):
            return ctx.enter_context(nc.semaphore(name))

        ids_sb = sb("ids_sb", [P, NT, F], i32)
        dense = sb("dense", [P, NT, D])
        emb = sb("emb", [P, 2, F, D])
        vecT = sb("vecT", [P, B, QUAD])
        pairs = sb("pairs", [P, NC, B])
        w1_pair = sb("w1_pair", [P, NC, H1])
        w1_dense = sb("w1_dense", [P, 2, H1])
        w1_sum = sb("w1_sum", [P, H1])
        w2 = sb("w2", [P, N1, H2])
        w3 = sb("w3", [P, N2])
        b2 = sb("b2", [P, N2])
        h1T = sb("h1T", [P, N1, B])
        h2T = sb("h2T", [P, N2, B])
        y = sb("y", [1, P, NT])
        ident = sb("ident", [P, P])
        row_int = sb("row_int", [HP, HC], i32)
        row_of = sb("row_of", [HP, HC])
        hot_ids = sb("hot_ids", [P, 2, B], i32)
        hot_idh = sb("hot_idh", [HP, 2, B], fp16)
        one_hot = sb("one_hot", [HP, 2, HC, B], bf16)
        hot_tab = sb("hot_tab", [HP, 2, HC, D])
        hot_rest = sb("hot_rest", [HP, HC, D])
        hot_part = sb("hot_part", [HP, 2, 3, HC, D], bf16)

        tp = [ps(f"tp{i}", [P, 4, P]) for i in range(2)]
        gram = [ps(f"gram{i}", [P, GPB, P]) for i in range(2)]
        mlp1 = ps("mlp1", [P, N1, P])
        mlp2 = ps("mlp2", [P, 4, P])

        ids_in = sem("ids_in")
        dense_in = sem("dense_in")
        gathered = [[sem(f"gathered{t}_{q}") for q in range(NQ)] for t in range(NT)]
        hot_ids_in = [sem(f"hot_ids_in{k}") for k in range(NH)]
        hot_tab_in = [sem(f"hot_tab_in{k}") for k in range(NH)]
        rows_int = sem("rows_int")
        rows_set = sem("rows_set")
        idh_set = sem("idh_set")
        one_hot_set = sem("one_hot_set")
        high_set = sem("high_set")
        rest_set = sem("rest_set")
        mid_set = sem("mid_set")
        low_set = sem("low_set")
        hot_done = sem("hot_done")
        hot_set = sem("hot_set")
        w1_in = sem("w1_in")
        wd_in = sem("wd_in")
        w23_in = sem("w23_in")
        w1_zero = sem("w1_zero")
        pads_set = sem("pads_set")
        ident_zero = sem("ident_zero")
        ident_set = sem("ident_set")
        wsum_set = sem("wsum_set")
        transposed = sem("transposed")
        vec_set = sem("vec_set")
        gram_done = sem("gram_done")
        pairs_act = sem("pairs_act")
        pairs_dve = sem("pairs_dve")
        mlp1_done = sem("mlp1_done")
        h1_act = sem("h1_act")
        h1_dve = sem("h1_dve")
        mlp2_done = sem("mlp2_done")
        h2_set = sem("h2_set")
        mlp3_done = sem("mlp3_done")
        y_set = sem("y_set")
        y_out = sem("y_out")

        block = ctx.enter_context(nc.Block())

        @block.sync
        def _(sp):
            sp.dma_start(ids_sb[:], ids.rearrange("(p t) f -> p t f", t=NT)).then_inc(ids_in, 16)

            def load_hot(k):
                table = tables[HOT[k]].rearrange("(p c) d -> p c d", c=HC)
                if k >= 2:
                    sp.wait_ge(idh_set, k - 1)
                col = ids_cols[HOT[k]:HOT[k] + 1, :]
                sp.dma_start(hot_ids[:, k % 2, :], col.to_broadcast([P, B])).then_inc(hot_ids_in[k], 16)
                if k >= 2:
                    sp.wait_ge(rest_set, k - 1)
                sp.dma_start(hot_tab[0:HS, k % 2], table[0:HS]).then_inc(hot_tab_in[k], 16)
                sp.dma_start(hot_tab[HS:HP, k % 2], table[HS:HP]).then_inc(hot_tab_in[k], 16)

            load_hot(0)
            load_hot(1)
            sp.dma_start(dense[:], r_dense_features.rearrange("(p t) d -> p t d", t=NT)).then_inc(dense_in, 16)
            sp.dma_start(w1_dense[:, 0], W_top1[0:D, :]).then_inc(wd_in, 16)
            sp.dma_start(w1_dense[:, 1], W_top1[W_top1.shape[0] - D:, :]).then_inc(wd_in, 16)
            for k in range(2, NH):
                load_hot(k)
            sp.wait_ge(w1_zero, 1)
            row = D + F
            for i in range(F):
                j, c = i % SPG, i // SPG
                if i < F - 1:
                    n = F - 1 - i
                    sp.dma_start(w1_pair[QUAD * j + i + 1:QUAD * j + F, c, :],
                                 W_top1[row:row + n, :]).then_inc(w1_in, 16)
                    row += n
            for j in range(SPG):
                n = width(j)
                sp.dma_start(w1_pair[QUAD * j + DENSE:QUAD * j + DENSE + 1, 0:n, :],
                             W_top1[D + j:D + j + SPG * (n - 1) + 1:SPG, :].rearrange("(o c) n -> o c n", o=1)
                             ).then_inc(w1_in, 16)
            sp.dma_start(w1_pair[ONE:ONE + 1, 0, :], b_top1.rearrange("(o n) -> o n", o=1)).then_inc(w1_in, 16)
            sp.dma_start(w2[:], W_top2.rearrange("(k p) n -> p k n", p=P)).then_inc(w23_in, 16)
            with nc.allow_non_contiguous_dma(reason="two short columns"):
                sp.dma_start(w3[:], W_top3.rearrange("(k p) o -> p (k o)", p=P)).then_inc(w23_in, 16)
                sp.dma_start(b2[:], b_top2.rearrange("(k p) -> p k", p=P)).then_inc(w23_in, 16)
            sp.wait_ge(y_set, NT)
            sp.dma_start(out.rearrange("(o b) n -> o (b n)", o=1), y[:].rearrange("o p t -> o (p t)")).then_inc(y_out, 16)
            sp.wait_ge(y_out, 16)

        W1_LOADS = (F - 1) + SPG + 1

        @block.gpsimd
        def _(pool):
            nc.gpsimd.memset(ident[:], 0.0).then_inc(ident_zero, 1)
            pool.wait_ge(ident_zero, 1)
            nc.gpsimd.affine_select(out=ident[:], in_=ident[:], compare_op=ALU.not_equal, fill=1.0,
                                    base=0, pattern=[[-1, P]], channel_multiplier=1).then_inc(ident_set, 1)
            nc.gpsimd.iota(row_int[:], [[1, HC]], base=0, channel_multiplier=HC).then_inc(rows_int, 1)
            pool.wait_ge(ids_in, 16)
            for t in range(NT):
                for q, slots in enumerate(SLOTS):
                    if t >= 2:
                        pool.wait_ge(transposed, (t - 2) * NQ + q + 1)
                    for f in slots:
                        if f == DENSE:
                            continue
                        nc.gpsimd.indirect_dma_start(emb[:, t % 2, f, :], None, tables[f],
                                                     bass.IndirectOffsetOnAxis(ids_sb[:, t, f:f + 1], 0)
                                                     ).then_inc(gathered[t][q], 16)

        def hot_psum(k):
            return gram[k // 2 % 2][:, 4 * (k % 2):4 * (k % 2) + 4, :]

        def h1_psum(t, half):
            return (tp[0][:, 0:2] if t == NT - 1 and half else mlp1[:, 2 * half:2 * half + 2])

        def h2_psum(t, k):
            return (tp[1][:, 0] if t == NT - 1 and k else mlp2[:, k])

        def pair_copy(engine, t, g, s, j):
            n = width(j)
            src = gram[(t * NG + g) % 2][QUAD * s:QUAD * s + NV, :, s * F + j:s * F + j + SPG * (n - 1) + 1:SPG]
            b0 = t * P + g * GPB * SPG + s
            dst = pairs[QUAD * j:QUAD * j + NV, 0:n, b0:b0 + SPG * (GPB - 1) + 1:SPG].rearrange("p c g -> p g c")
            return engine(dst, src)

        @block.scalar
        def _(act):
            def split_hot(k):
                act.wait_ge(hot_tab_in[k], 32)
                if k >= 2:
                    act.wait_ge(hot_done, k - 1)
                nc.scalar.copy(hot_part[:, k % 2, 0], hot_tab[:, k % 2]).then_inc(high_set, 1)
                act.wait_ge(rest_set, k + 1)
                nc.scalar.copy(hot_part[:, k % 2, 1], hot_rest[:]).then_inc(mid_set, 1)

            def hot_out(k):
                act.wait_ge(hot_done, k + 1)
                nc.scalar.copy(vecT[:, :, HOT[k]], hot_psum(k).rearrange("d t p -> d (t p)")).then_inc(hot_set, 1)

            def slots_out(t, q):
                act.wait_ge(transposed, t * NQ + q + 1)
                for at, slot, n in runs(q):
                    last = nc.scalar.copy(vecT[:, t * P:(t + 1) * P, slot:slot + n].rearrange("p b s -> p s b"),
                                          tp[(t * NQ + q) % 2][:, at:at + n, :])
                last.then_inc(vec_set, 1)

            def pairs_out(t, g):
                act.wait_ge(gram_done, t * NG + g + 1)
                for s in range(2):
                    for j in range(SPG):
                        last = pair_copy(nc.scalar.copy, t, g, s, j)
                last.then_inc(pairs_act, 1)

            def h2_out(t, k):
                act.wait_ge(mlp2_done, N2 * t + k + 1)
                act.wait_ge(w23_in, 48)
                nc.scalar.activation(h2T[:, k, t * P:(t + 1) * P], h2_psum(t, k), ACT.Relu,
                                     bias=b2[:, k:k + 1]).then_inc(h2_set, 1)

            split_hot(0)
            split_hot(1)
            slots_out(0, 0)
            hot_out(0)
            split_hot(2)
            slots_out(0, 1)
            hot_out(1)
            split_hot(3)
            slots_out(0, 2)
            slots_out(0, 3)
            hot_out(2)
            slots_out(0, 4)
            hot_out(3)
            slots_out(0, 5)
            act.wait_ge(pads_set, 2)
            for t in range(1, NT):
                slots_out(t, 0)
                pairs_out(t - 1, 0)
                pairs_out(t - 1, 1)
                slots_out(t, 1)
                pairs_out(t - 1, 2)
                pairs_out(t - 1, 3)
                slots_out(t, 2)
                slots_out(t, 3)
                for k in range(N2):
                    h2_out(t - 1, k)
                slots_out(t, 4)
                slots_out(t, 5)
            for g in range(NG):
                pairs_out(NT - 1, g)
            act.wait_ge(mlp1_done, 2 * NT - 1)
            nc.scalar.activation(h1T[:, 0:2, (NT - 1) * P:], h1_psum(NT - 1, 0), ACT.Relu).then_inc(h1_act, 1)
            for k in range(N2):
                h2_out(NT - 1, k)

        @block.vector
        def _(dve):
            dve.wait_ge(rows_int, 1)
            nc.vector.tensor_copy(row_of[:], row_int[:]).then_inc(rows_set, 1)
            dve.wait_ge(rows_set, 1)

            def make_one_hot(k):
                dve.wait_ge(hot_ids_in[k], 16)
                nc.vector.tensor_copy(hot_idh[:, k % 2], hot_ids[0:HP, k % 2]).then_inc(idh_set, 1)
                dve.wait_ge(idh_set, k + 1)
                if k >= 2:
                    dve.wait_ge(hot_done, k - 1)
                for c in range(HC):
                    last = nc.vector.tensor_scalar(one_hot[:, k % 2, c], hot_idh[:, k % 2],
                                                   row_of[:, c:c + 1], None, ALU.is_equal)
                last.then_inc(one_hot_set, 1)

            def split_rest(k):
                if k > 0:
                    dve.wait_ge(low_set, k)
                dve.wait_ge(high_set, k + 1)
                nc.vector.tensor_tensor(hot_rest[:], hot_tab[:, k % 2], hot_part[:, k % 2, 0],
                                        ALU.subtract).then_inc(rest_set, 1)

            def split_low(k):
                dve.wait_ge(mid_set, k + 1)
                nc.vector.tensor_tensor(hot_part[:, k % 2, 2], hot_rest[:], hot_part[:, k % 2, 1],
                                        ALU.subtract).then_inc(low_set, 1)

            split_rest(0)
            make_one_hot(0)
            split_low(0)
            split_rest(1)
            make_one_hot(1)
            split_low(1)
            nc.vector.memset(w1_pair[:], 0.0).then_inc(w1_zero, 1)
            split_rest(2)
            make_one_hot(2)
            split_low(2)
            nc.vector.memset(vecT[:, :, NV:QUAD], 0.0).then_inc(pads_set, 1)
            split_rest(3)
            make_one_hot(3)
            split_low(3)
            nc.vector.memset(pairs[:], 1.0).then_inc(pads_set, 1)
            dve.wait_ge(wd_in, 32)
            nc.vector.tensor_tensor(w1_sum[:], w1_dense[:, 0], w1_dense[:, 1], ALU.add).then_inc(wsum_set, 1)
            dve.wait_ge(pads_set, 2)
            for t in range(NT):
                for g in range(NG):
                    dve.wait_ge(gram_done, t * NG + g + 1)
                    for s in range(2, SPG):
                        for j in range(SPG):
                            last = pair_copy(nc.vector.tensor_copy, t, g, s, j)
                    last.then_inc(pairs_dve, 1)
                dve.wait_ge(mlp1_done, 2 * (t + 1))
                for half in range(2):
                    if half == 1 or t < NT - 1:
                        last = nc.vector.tensor_scalar_max(h1T[:, 2 * half:2 * half + 2, t * P:(t + 1) * P],
                                                           h1_psum(t, half), 0.0)
                last.then_inc(h1_dve, 1)
                dve.wait_ge(mlp3_done, t + 1)
                nc.vector.tensor_copy(y[:, :, t], mlp2[0:1, N2, :]).then_inc(y_set, 1)

        @block.tensor
        def _(pe):
            def transposes(t, q):
                k = t * NQ + q
                if k >= 2:
                    pe.wait_ge(vec_set, k - 1)
                pe.wait_ge(gathered[t][q], 16 * sum(slot != DENSE for slot in SLOTS[q]))
                for at, slot in enumerate(SLOTS[q]):
                    src = dense[:, t, :] if slot == DENSE else emb[:, t % 2, slot, :]
                    last = nc.tensor.transpose(tp[k % 2][:, at, :], src, ident[:])
                last.then_inc(transposed, 1)

            def look_up(k):
                pe.wait_ge(one_hot_set, k + 1)
                pe.wait_ge(low_set, k + 1)
                if k >= 4:
                    pe.wait_ge(hot_set, k - 3)
                steps = [(part, c) for part in range(3) for c in range(HC)]
                for part, c in steps:
                    last = nc.tensor.matmul(hot_psum(k), hot_part[:, k % 2, part, c, :], one_hot[:, k % 2, c],
                                            start=(part, c) == steps[0], stop=(part, c) == steps[-1])
                last.then_inc(hot_done, 1)

            def grams(t, g):
                k = t * NG + g
                pe.wait_ge(vec_set, NQ * (t + 1))
                if k == 0:
                    pe.wait_ge(hot_set, NH)
                    pe.wait_ge(pads_set, 1)
                if k >= 2:
                    pe.wait_ge(pairs_act, k - 1)
                    pe.wait_ge(pairs_dve, k - 1)
                for i in range(GPB):
                    b0 = t * P + (g * GPB + i) * SPG
                    last = nc.tensor.matmul(gram[k % 2][0:M, i, 0:SPG * F],
                                            vecT[:, b0:b0 + SPG, :].rearrange("p b s -> p (b s)")[:, 0:M],
                                            vecT[:, b0:b0 + SPG, 0:F], start=True, stop=True)
                last.then_inc(gram_done, 1)

            def layer1_dense(t):
                cols = slice(t * P, (t + 1) * P)
                if t > 0:
                    pe.wait_ge(h1_dve, t)
                else:
                    pe.wait_ge(wsum_set, 1)
                for n in range(N1):
                    fresh = n == 0 or (t == NT - 1 and n == 2)
                    if fresh and n == 2:
                        pe.wait_ge(vec_set, NQ * NT)
                    nc.tensor.matmul(h1_psum(t, n // 2)[:, n % 2], w1_sum[:, n * P:(n + 1) * P],
                                     vecT[:, cols, DENSE], start=fresh, stop=False, skip_group_check=True)

            def layer1_pairs(t, half):
                if t == 0:
                    pe.wait_ge(w1_in, 16 * W1_LOADS)
                pe.wait_ge(pairs_act, NG * (t + 1))
                pe.wait_ge(pairs_dve, NG * (t + 1))
                cols = slice(t * P, (t + 1) * P)
                for n in (2 * half, 2 * half + 1):
                    for c in range(NC):
                        rows = QUAD * min(SPG, F - c * SPG)
                        last = nc.tensor.matmul(h1_psum(t, half)[:, n % 2], w1_pair[0:rows, c, n * P:(n + 1) * P],
                                                pairs[0:rows, c, cols], start=False, stop=c == NC - 1,
                                                skip_group_check=True)
                last.then_inc(mlp1_done, 1)

            def layer2(t):
                cols = slice(t * P, (t + 1) * P)
                if t > 0:
                    pe.wait_ge(y_set, t)
                else:
                    pe.wait_ge(w23_in, 48)
                if t == NT - 1:
                    pe.wait_ge(h1_act, 1)
                else:
                    pe.wait_ge(h1_dve, t + 1)
                for n in range(N2):
                    for k in range(N1):
                        if t == NT - 1 and (n, k) == (0, 2):
                            pe.wait_ge(h1_dve, NT)
                        last = nc.tensor.matmul(h2_psum(t, n), w2[:, k, n * P:(n + 1) * P], h1T[:, k, cols],
                                                start=k == 0, stop=k == N1 - 1)
                        if k == N1 - 1:
                            if t == NT - 1:
                                last.then_inc(mlp2_done, 1)
                            elif n == N2 - 1:
                                last.then_inc(mlp2_done, N2)

            def layer3(t):
                cols = slice(t * P, (t + 1) * P)
                for k in range(N2):
                    pe.wait_ge(h2_set, N2 * t + (k + 1 if t == NT - 1 else N2))
                    last = nc.tensor.matmul(mlp2[0:1, N2, :], w3[:, k:k + 1], h2T[:, k, cols],
                                            start=k == 0, stop=k == N2 - 1)
                last.then_inc(mlp3_done, 1)

            pe.wait_ge(ident_set, 1)
            pe.wait_ge(dense_in, 16)
            look_up(0)
            transposes(0, 0)
            look_up(1)
            transposes(0, 1)
            look_up(2)
            transposes(0, 2)
            transposes(0, 3)
            look_up(3)
            transposes(0, 4)
            transposes(0, 5)
            for t in range(1, NT):
                transposes(t, 0)
                grams(t - 1, 0)
                grams(t - 1, 1)
                transposes(t, 1)
                grams(t - 1, 2)
                grams(t - 1, 3)
                layer1_dense(t - 1)
                transposes(t, 2)
                layer1_pairs(t - 1, 0)
                layer1_pairs(t - 1, 1)
                transposes(t, 3)
                layer2(t - 1)
                transposes(t, 4)
                layer3(t - 1)
                transposes(t, 5)
            for g in range(NG):
                grams(NT - 1, g)
            layer1_dense(NT - 1)
            layer1_pairs(NT - 1, 0)
            layer1_pairs(NT - 1, 1)
            layer2(NT - 1)
            layer3(NT - 1)


def kernel(**inputs):
    import numpy as np
    import concourse.bacc as bacc
    from concourse import mybir
    from concourse.bass_utils import run_bass_kernel_spmd

    nc = bacc.Bacc("TRN2", target_bir_lowering=False, num_devices=1)
    arrays, aps = {}, {}
    for name, value in inputs.items():
        a = np.ascontiguousarray(value)
        arrays[f"in_{name}"] = a
        aps[name] = nc.dram_tensor(f"in_{name}", a.shape, mybir.dt.from_np(a.dtype), kind="ExternalInput").ap()
    batch, features = inputs["ids"].shape
    cols = np.ascontiguousarray(np.asarray(inputs["ids"]).reshape(128, batch // 128, features)
                                .transpose(2, 1, 0).reshape(features, batch))
    arrays["in_ids_cols"] = cols
    ids_cols = nc.dram_tensor("in_ids_cols", cols.shape, mybir.dt.from_np(cols.dtype), kind="ExternalInput").ap()
    out = nc.dram_tensor("out_y", (batch, 1), mybir.dt.float32, kind="ExternalOutput").ap()
    dlrm_tower(nc, aps["r_dense_features"], aps["ids"], ids_cols, [aps[f"tbl_{f}"] for f in range(features)],
               aps["W_top1"], aps["b_top1"], aps["W_top2"], aps["b_top2"], aps["W_top3"], out)
    return run_bass_kernel_spmd(nc, [arrays], core_ids=[0]).results[0]["out_y"]
```

```python
def dlrm_tower(nc, r_dense_features, ids, ids_cols, tables, W_top1, b_top1, W_top2, b_top2, W_top3, out):
    import concourse.bass as bass
    from concourse import mybir
    from contextlib import ExitStack

    fp32 = mybir.dt.float32
    i32 = mybir.dt.int32
    fp16 = mybir.dt.float16
    bf16 = mybir.dt.bfloat16
    fp32r = mybir.dt.float32r
    ALU = mybir.AluOpType
    ACT = mybir.ActivationFunctionType

    P = 128
    B, F = ids.shape
    D = tables[0].shape[1]
    H1, H2 = W_top2.shape
    NT = B // P
    QUAD = 32
    SPG = P // QUAD
    NV = F + 1
    DENSE = F
    GPT = P // SPG
    GPB = 8
    NG = GPT // GPB
    NC = F // SPG
    NK = NC * SPG
    NX = F - NK
    assert NX == 2
    N1 = H1 // P
    N2 = H2 // P
    REPEATS = {DENSE: NV, F - 1: NV + 1}
    PAD = NV + NX
    M = QUAD * (SPG - 1) + PAD
    ONE = QUAD * (SPG - 1) + NV

    HOT = [25, 24, 14, 11, 7, 3]
    HC = 8
    HP = tables[HOT[0]].shape[0] // HC
    assert all(tables[f].shape[0] == HP * HC <= 2048 for f in HOT) and HP <= P
    HS = HP // 16 * 16
    HA = 1
    HV = HC - HA
    LATE_FROM = 1
    LATE = [2]
    HOT = HOT + LATE
    assert len(LATE) <= 1
    LOADS = 3
    WARM = 10
    NH = len(HOT)
    NF = NH - len(LATE)
    COLD = [f for f in range(F) if f not in HOT or f in LATE]

    SLOTS = [[21, 22, 23, DENSE], [17, 18, 19, 20], [12, 13, 15, 16], [8, 9, 10], [4, 5, 6], [1, 2], [0]]
    NQ = len(SLOTS)
    AFTER = [[], [0], [1], [2, 3], [4, 5], [6]]
    assert len(AFTER) == NF and sum(AFTER, []) == list(range(NQ))
    assert sorted(sum(SLOTS, [f for f in HOT if f not in LATE])) == list(range(NV))

    def slots_of(t, q):
        return [slot for slot in SLOTS[q] if t < LATE_FROM or slot not in LATE]

    def looked_up(k):
        return slice(LATE_FROM * P if HOT[k] in LATE else 0, B)

    def runs(t, q):
        found = []
        for at, slot in enumerate(slots_of(t, q)):
            if found and found[-1][1] + found[-1][2] == slot:
                found[-1][2] += 1
            else:
                found.append([at, slot, 1])
        return found

    with ExitStack() as ctx:
        def sb(name, shape, dt=fp32):
            return ctx.enter_context(nc.sbuf_tensor(name, shape, dt))

        def ps(name, shape):
            return ctx.enter_context(nc.psum_tensor(name, shape, fp32))

        def sem(name):
            return ctx.enter_context(nc.semaphore(name))

        ids_sb = sb("ids_sb", [P, NT, F], i32)
        dense = sb("dense", [P, NT, D])
        emb = sb("emb", [P, 2, len(COLD), D])
        vecT = sb("vecT", [P, B, QUAD])
        pairs = sb("pairs", [P, NC, B])
        w1_pair = sb("w1_pair", [P, NC, H1])
        w1_dense = sb("w1_dense", [P, 2, H1])
        w1_sum = sb("w1_sum", [P, H1])
        w2 = sb("w2", [P, N1, H2])
        w3 = sb("w3", [P, N2])
        b2 = sb("b2", [P, N2])
        h1T = sb("h1T", [P, N1, B])
        h2T = sb("h2T", [P, N2, B])
        y = sb("y", [1, P, NT])
        ones_row = sb("ones_row", [1, B])
        ident = sb("ident", [P, P])
        row_int = sb("row_int", [HP, 1], i32)
        row_of = sb("row_of", [HP, 1])
        hot_ids = sb("hot_ids", [P, LOADS, B], i32)
        hot_rel = sb("hot_rel", [HP, 2, B], fp16)
        hot_far = sb("hot_far", [HP, B], bf16)
        one_hot = sb("one_hot", [HP, 2, HC, B], fp32r)
        hot_tab = sb("hot_tab", [HP, LOADS, HC, D])
        hot_part = sb("hot_part", [HP, 2, 2, HC, D], fp32r)
        filling = sb("filling", [P, 2 + HA])

        tp = [ps(f"tp{i}", [P, 4, P]) for i in range(2)]
        gram = [ps(f"gram{i}", [P, GPB, P]) for i in range(2)]
        mlp = [ps(f"mlp{i}", [P, 4, P]) for i in range(2)]

        ids_in = sem("ids_in")
        dense_in = sem("dense_in")
        gathered = [[sem(f"gathered{t}_{q}") for q in range(NQ)] for t in range(NT)]
        hot_ids_in = [sem(f"hot_ids_in{k}") for k in range(NH)]
        hot_tab_in = [sem(f"hot_tab_in{k}") for k in range(NH)]
        rows_int = sem("rows_int")
        rows_set = sem("rows_set")
        rel_set = sem("rel_set")
        one_hot_dve = sem("one_hot_dve")
        far_set = sem("far_set")
        one_hot_act = sem("one_hot_act")
        high_set = sem("high_set")
        first_high_set = sem("first_high_set")
        filling_set = sem("filling_set")
        low_set = sem("low_set")
        hot_done = sem("hot_done")
        hot_set = sem("hot_set")
        w1_in = sem("w1_in")
        wd_in = sem("wd_in")
        w23_in = sem("w23_in")
        w1_zero = sem("w1_zero")
        gaps_in = sem("gaps_in")
        ones_set = sem("ones_set")
        pads_set = sem("pads_set")
        ident_zero = sem("ident_zero")
        ident_set = sem("ident_set")
        wsum_set = sem("wsum_set")
        transposed = sem("transposed")
        vec_set = sem("vec_set")
        gram_done = sem("gram_done")
        extra_act = sem("extra_act")
        extra_dve = sem("extra_dve")
        pairs_act = sem("pairs_act")
        pairs_dve = sem("pairs_dve")
        mlp1_done = sem("mlp1_done")
        h1_act = sem("h1_act")
        h1_dve = sem("h1_dve")
        mlp2_done = sem("mlp2_done")
        h2_set = sem("h2_set")
        mlp3_done = sem("mlp3_done")
        y_set = sem("y_set")
        y_out = sem("y_out")

        block = ctx.enter_context(nc.Block())

        @block.sync
        def _(sp):
            sp.dma_start(ids_sb[:], ids.rearrange("(p t) f -> p t f", t=NT)).then_inc(ids_in, 16)

            def load_hot(k):
                table = tables[HOT[k]].rearrange("(p c) d -> p c d", c=HC)
                if k >= LOADS:
                    sp.wait_ge(rel_set, k - LOADS + 1)
                col = ids_cols[HOT[k]:HOT[k] + 1, :]
                sp.dma_start(hot_ids[:, k % LOADS, :], col.to_broadcast([P, B])).then_inc(hot_ids_in[k], 16)
                if k >= LOADS:
                    sp.wait_ge(low_set, k - LOADS + 1)
                sp.dma_start(hot_tab[0:HS, k % LOADS], table[0:HS]).then_inc(hot_tab_in[k], 16)
                sp.dma_start(hot_tab[HS:HP, k % LOADS], table[HS:HP]).then_inc(hot_tab_in[k], 16)

            for k in range(LOADS):
                load_hot(k)
            sp.dma_start(dense[:], r_dense_features.rearrange("(p t) d -> p t d", t=NT)).then_inc(dense_in, 16)
            sp.dma_start(w1_dense[:, 0], W_top1[0:D, :]).then_inc(wd_in, 16)
            sp.dma_start(w1_dense[:, 1], W_top1[W_top1.shape[0] - D:, :]).then_inc(wd_in, 16)
            sp.wait_ge(w1_zero, 1)
            row = D + F
            for i in range(NK):
                if i % 5 == 0 and LOADS + i // 5 < NH:
                    load_hot(LOADS + i // 5)
                j, c = i % SPG, i // SPG
                n = F - 1 - i
                sp.dma_start(w1_pair[QUAD * j + i + 1:QUAD * j + F, c, :], W_top1[row:row + n, :]).then_inc(w1_in, 16)
                row += n
            for j in range(SPG):
                sp.dma_start(w1_pair[QUAD * j + DENSE:QUAD * j + DENSE + 1, :, :],
                             W_top1[D + j:D + NK:SPG, :].rearrange("(o c) n -> o c n", o=1)).then_inc(w1_in, 16)
            sp.dma_start(w1_pair[NV:NV + 1, 0:NX, :],
                         W_top1[D + NK:D + F, :].rearrange("(o c) n -> o c n", o=1)).then_inc(w1_in, 16)
            sp.dma_start(w1_pair[NV + 1:NV + 2, 0, :], W_top1[row:row + 1, :]).then_inc(w1_in, 16)
            sp.dma_start(w1_pair[ONE:ONE + 1, NC - 1, :], b_top1.rearrange("(o n) -> o n", o=1)).then_inc(w1_in, 16)
            for j in range(1, SPG):
                gap = slice(QUAD * j + NV, QUAD * (j + 1))
                chunks = NC - 1 if j == SPG - 1 else NC
                sp.dma_start(pairs[gap, 0:chunks, :], w1_pair[gap, 0:chunks, :]).then_inc(gaps_in, 16)
            sp.dma_start(pairs[NV:QUAD, NX:NC, :], w1_pair[NV:QUAD, NX:NC, :]).then_inc(gaps_in, 16)
            sp.dma_start(pairs[PAD:QUAD, 0:NX, :], w1_pair[PAD:QUAD, 0:NX, :]).then_inc(gaps_in, 16)
            sp.dma_start(pairs[ONE + 1:P, NC - 1, :], w1_pair[ONE + 1:P, NC - 1, :]).then_inc(gaps_in, 16)
            sp.wait_ge(ones_set, 1)
            sp.dma_start(pairs[ONE:ONE + 1, NC - 1, :], ones_row[:]).then_inc(gaps_in, 16)
            sp.dma_start(w2[:], W_top2.rearrange("(k p) n -> p k n", p=P)).then_inc(w23_in, 16)
            with nc.allow_non_contiguous_dma(reason="two short columns"):
                sp.dma_start(w3[:], W_top3.rearrange("(k p) o -> p (k o)", p=P)).then_inc(w23_in, 16)
                sp.dma_start(b2[:], b_top2.rearrange("(k p) -> p k", p=P)).then_inc(w23_in, 16)
            sp.wait_ge(y_set, NT)
            sp.dma_start(out.rearrange("(o b) n -> o (b n)", o=1), y[:].rearrange("o p t -> o (p t)")).then_inc(y_out, 16)
            sp.wait_ge(y_out, 16)

        W1_LOADS = NK + SPG + 3
        GAP_LOADS = SPG + 3

        @block.gpsimd
        def _(pool):
            nc.gpsimd.memset(ident[:], 0.0).then_inc(ident_zero, 1)
            pool.wait_ge(ident_zero, 1)
            nc.gpsimd.affine_select(out=ident[:], in_=ident[:], compare_op=ALU.not_equal, fill=1.0,
                                    base=0, pattern=[[-1, P]], channel_multiplier=1).then_inc(ident_set, 1)
            nc.gpsimd.iota(row_int[:], [[0, 1]], base=0, channel_multiplier=-HC).then_inc(rows_int, 1)
            nc.gpsimd.memset(ones_row[:], 1.0).then_inc(ones_set, 1)
            pool.wait_ge(ids_in, 16)
            for t in range(NT):
                for q in range(NQ):
                    if t >= 2:
                        pool.wait_ge(transposed, (t - 2) * NQ + q + 1)
                    for f in slots_of(t, q):
                        if f == DENSE:
                            continue
                        nc.gpsimd.indirect_dma_start(emb[:, t % 2, COLD.index(f), :], None, tables[f],
                                                     bass.IndirectOffsetOnAxis(ids_sb[:, t, f:f + 1], 0)
                                                     ).then_inc(gathered[t][q], 16)

        def hot_psum(k):
            n = (looked_up(k).stop - looked_up(k).start) // P
            if k >= NF:
                return gram[0][:, 0:n, :]
            return gram[k // 2 % 2][:, 4 * (k % 2):4 * (k % 2) + n, :]

        def h1_psum(half):
            return mlp[half][:, 0:2]

        def h2_psum(t, n):
            return tp[1][:, 0] if t == NT - 1 and n else mlp[0][:, 2 + n]

        y_psum = mlp[1][0:1, 2]

        def block_of(t, g, s, rows, first, n):
            return gram[(t * NG + g) % 2][QUAD * s:QUAD * s + rows, first:first + n, s * F:(s + 1) * F]

        def samples(t, g, s, first, n):
            at = t * P + (g * GPB + first) * SPG + s
            return slice(at, at + SPG * (n - 1) + 1, SPG)

        def copy_extra(copy, t, g, s, first, n):
            return copy(pairs[0:PAD, 0:NX, samples(t, g, s, first, n)].rearrange("p c g -> p g c"),
                        block_of(t, g, s, PAD, first, n)[:, :, NK:F])

        def copy_columns(copy, t, g, s, j, first, n):
            return copy(pairs[QUAD * j:QUAD * j + NV, :, samples(t, g, s, first, n)].rearrange("p c g -> p g c"),
                        block_of(t, g, s, NV, first, n)[:, :, j:NK:SPG])

        def pieces(t, g):
            n = GPB // 2 if (t, g) == (NT - 1, NG - 1) else GPB
            return [(first, n) for first in range(0, GPB, n)]

        def act_samples(t, g, piece):
            return 3 if len(pieces(t, g)) == 2 and piece == 0 else 2

        @block.scalar
        def _(act):
            def relative(k):
                cols = looked_up(k)
                act.wait_ge(hot_ids_in[k], 16)
                if k >= 2:
                    act.wait_ge(one_hot_dve, HV * (k - 1))
                    act.wait_ge(far_set, HA * (k - 1))
                nc.scalar.activation(hot_rel[:, k % 2, cols], hot_ids[0:HP, k % LOADS, cols], ACT.Identity,
                                     bias=row_of[:]).then_inc(rel_set, 1)

            def split_high(k):
                act.wait_ge(hot_tab_in[k], 32)
                if k >= 2:
                    act.wait_ge(hot_done, k - 1)
                chunks = slice(0, HC)
                if k == 0:
                    nc.scalar.copy(hot_part[:, 0, 0, 0:HC // 2], hot_tab[:, 0, 0:HC // 2]).then_inc(first_high_set, 1)
                    chunks = slice(HC // 2, HC)
                nc.scalar.copy(hot_part[:, k % 2, 0, chunks], hot_tab[:, k % LOADS, chunks]).then_inc(high_set, 1)

            def one_hots(k):
                cols = looked_up(k)
                act.wait_ge(rel_set, k + 1)
                for a in range(HA):
                    done = k * HA + a
                    if done > 0:
                        act.wait_ge(one_hot_act, done)
                    nc.scalar.activation(hot_far[:, cols], hot_rel[:, k % 2, cols], ACT.Square,
                                         bias=filling[0:HP, 2 + a:3 + a]).then_inc(far_set, 1)
                    act.wait_ge(far_set, done + 1)
                    nc.scalar.activation(one_hot[:, k % 2, HV + a, cols], hot_far[:, cols], ACT.Relu,
                                         bias=filling[0:HP, 1:2], scale=-1.0).then_inc(one_hot_act, 1)

            def hot_out(k):
                act.wait_ge(hot_done, k + 1)
                for slot in (HOT[k], REPEATS.get(HOT[k])):
                    if slot is not None:
                        last = nc.scalar.copy(vecT[:, looked_up(k), slot], hot_psum(k).rearrange("d t p -> d (t p)"))
                last.then_inc(hot_set, 1)

            def slots_out(t, q):
                act.wait_ge(transposed, t * NQ + q + 1)
                for at, slot, n in runs(t, q):
                    last = nc.scalar.copy(vecT[:, t * P:(t + 1) * P, slot:slot + n].rearrange("p b s -> p s b"),
                                          tp[(t * NQ + q) % 2][:, at:at + n, :])
                for at, slot in enumerate(slots_of(t, q)):
                    if slot in REPEATS:
                        last = nc.scalar.copy(vecT[:, t * P:(t + 1) * P, REPEATS[slot]],
                                              tp[(t * NQ + q) % 2][:, at, :])
                last.then_inc(vec_set, 1)

            def pairs_out(t, g):
                copied = 2 * (t * NG + g)
                for piece, (first, n) in enumerate(pieces(t, g)):
                    mine = range(0, act_samples(t, g, piece))
                    copied += len(mine)
                    act.wait_ge(gram_done, t * NG + g + 1 + piece)
                    for s in mine:
                        copy_extra(nc.scalar.copy, t, g, s, first, n).then_inc(extra_act, 1)
                    for j in range(SPG - 1, -1, -1):
                        if j == 0:
                            act.wait_ge(extra_act, copied)
                        for s in mine:
                            last = copy_columns(nc.scalar.copy, t, g, s, j, first, n)
                last.then_inc(pairs_act, 1)

            def h1_out(t):
                act.wait_ge(mlp1_done, 2 * t + 1)
                nc.scalar.activation(h1T[:, 0:2, t * P:(t + 1) * P], h1_psum(0), ACT.Relu).then_inc(h1_act, 1)

            def h2_out(t, k):
                act.wait_ge(mlp2_done, N2 * t + k + 1)
                act.wait_ge(w23_in, 48)
                nc.scalar.activation(h2T[:, k, t * P:(t + 1) * P], h2_psum(t, k), ACT.Relu,
                                     bias=b2[:, k:k + 1]).then_inc(h2_set, 1)

            def looked_out(k):
                hot_out(k)
                for q in AFTER[k]:
                    slots_out(0, q)

            act.wait_ge(filling_set, 2 + HA)
            nc.scalar.copy(vecT[:, :, PAD:QUAD], filling[:, 0:1].to_broadcast([P, B, QUAD - PAD])).then_inc(pads_set, 1)
            act.wait_ge(rows_set, 1)
            relative(0)
            split_high(0)
            for k in range(NF):
                one_hots(k)
                if k + 1 < NH:
                    relative(k + 1)
                    split_high(k + 1)
                if k > 0:
                    looked_out(k - 1)
            looked_out(NF - 1)
            for k in range(NF, NH):
                one_hots(k)
            for t in range(1, NT):
                pairs_out(t - 1, 0)
                slots_out(t, 0)
                pairs_out(t - 1, 1)
                slots_out(t, 1)
                pairs_out(t - 1, 2)
                pairs_out(t - 1, 3)
                if t == 1:
                    for k in range(NF, NH):
                        hot_out(k)
                slots_out(t, 2)
                h1_out(t - 1)
                slots_out(t, 3)
                for q in range(4, NQ):
                    slots_out(t, q)
                for k in range(N2):
                    h2_out(t - 1, k)
            for g in range(NG):
                pairs_out(NT - 1, g)
            h1_out(NT - 1)
            for k in range(N2):
                h2_out(NT - 1, k)

        @block.vector
        def _(dve):
            nc.vector.memset(filling[:, 0:1], 0.0).then_inc(filling_set, 1)
            nc.vector.memset(filling[:, 1:2], 1.0).then_inc(filling_set, 1)
            for a in range(HA):
                nc.vector.memset(filling[:, 2 + a:3 + a], -float(HV + a)).then_inc(filling_set, 1)
            dve.wait_ge(rows_int, 1)
            nc.vector.tensor_copy(row_of[:], row_int[:]).then_inc(rows_set, 1)
            nc.vector.memset(w1_pair[:], 0.0).then_inc(w1_zero, 1)
            def one_hots(k):
                dve.wait_ge(rel_set, k + 1)
                if k >= 2:
                    dve.wait_ge(hot_done, k - 1)
                cols = looked_up(k)
                for c in range(HV):
                    nc.vector.tensor_scalar(one_hot[:, k % 2, c, cols], hot_rel[:, k % 2, cols], float(c), None,
                                            ALU.is_equal).then_inc(one_hot_dve, 1)

            def split_low(k):
                if k == 0:
                    dve.wait_ge(first_high_set, 1)
                dve.wait_ge(high_set, k + 1)
                nc.vector.tensor_tensor(hot_part[:, k % 2, 1], hot_tab[:, k % LOADS], hot_part[:, k % 2, 0],
                                        ALU.subtract).then_inc(low_set, 1)

            for k in range(NH):
                if k == NF:
                    dve.wait_ge(wd_in, 32)
                    nc.vector.tensor_tensor(w1_sum[:], w1_dense[:, 0], w1_dense[:, 1], ALU.add).then_inc(wsum_set, 1)
                one_hots(k)
                split_low(k)

            def pairs_out(t, g):
                copied = 2 * (t * NG + g)
                for piece, (first, n) in enumerate(pieces(t, g)):
                    mine = range(act_samples(t, g, piece), SPG)
                    copied += len(mine)
                    dve.wait_ge(gram_done, t * NG + g + 1 + piece)
                    for s in mine:
                        copy_extra(nc.vector.tensor_copy, t, g, s, first, n).then_inc(extra_dve, 1)
                    for j in range(SPG - 1, -1, -1):
                        if j == 0:
                            dve.wait_ge(extra_dve, copied)
                        for s in mine:
                            last = copy_columns(nc.vector.tensor_copy, t, g, s, j, first, n)
                last.then_inc(pairs_dve, 1)

            def h1_out(t):
                dve.wait_ge(mlp1_done, 2 * (t + 1))
                nc.vector.tensor_scalar_max(h1T[:, 2:4, t * P:(t + 1) * P], h1_psum(1), 0.0).then_inc(h1_dve, 1)

            def y_out_of(t):
                dve.wait_ge(mlp3_done, t + 1)
                nc.vector.tensor_copy(y[:, :, t], y_psum).then_inc(y_set, 1)

            for t in range(NT):
                for g in range(NG):
                    pairs_out(t, g)
                    if t > 0 and g == 0:
                        y_out_of(t - 1)
                h1_out(t)
            y_out_of(NT - 1)

        @block.tensor
        def _(pe):
            def transposes(t, q):
                k = t * NQ + q
                if k >= 2:
                    pe.wait_ge(vec_set, k - 1)
                pe.wait_ge(gathered[t][q], 16 * sum(slot != DENSE for slot in slots_of(t, q)))
                for at, slot in enumerate(slots_of(t, q)):
                    if slot == DENSE and t == 0:
                        pe.wait_ge(dense_in, 16)
                    src = dense[:, t, :] if slot == DENSE else emb[:, t % 2, COLD.index(slot), :]
                    last = nc.tensor.transpose(tp[k % 2][:, at, :], src, ident[:])
                last.then_inc(transposed, 1)

            def look_up(k):
                if k == 0:
                    pe.wait_ge(first_high_set, 1)
                else:
                    pe.wait_ge(high_set, k + 1)
                if k >= 4:
                    pe.wait_ge(hot_set, k - 3)
                if k >= NF:
                    pe.wait_ge(pairs_act, NG - 1)
                    pe.wait_ge(pairs_dve, NG - 1)
                steps = [(part, c) for part in range(2) for c in range(HC)]
                for part, c in steps:
                    if (k, part, c) == (0, 0, HC // 2):
                        pe.wait_ge(high_set, 1)
                    if part == 0 and c < HV:
                        pe.wait_ge(one_hot_dve, HV * k + c + 1)
                    elif part == 0:
                        pe.wait_ge(one_hot_act, HA * k + c - HV + 1)
                    elif c == 0:
                        pe.wait_ge(low_set, k + 1)
                    last = nc.tensor.matmul(hot_psum(k), hot_part[:, k % 2, part, c, :],
                                            one_hot[:, k % 2, c, looked_up(k)],
                                            start=(part, c) == steps[0], stop=(part, c) == steps[-1])
                last.then_inc(hot_done, 1)

            def grams(t, g):
                k = t * NG + g
                pe.wait_ge(vec_set, NQ * (t + 1))
                if k == 0:
                    pe.wait_ge(hot_set, NF)
                    pe.wait_ge(pads_set, 1)
                elif k == NG * LATE_FROM:
                    pe.wait_ge(hot_set, NH)
                if k >= 2:
                    pe.wait_ge(pairs_act, k - 1)
                    pe.wait_ge(pairs_dve, k - 1)
                for i in range(GPB):
                    b0 = t * P + (g * GPB + i) * SPG
                    last = nc.tensor.matmul(gram[k % 2][0:M, i, 0:SPG * F],
                                            vecT[:, b0:b0 + SPG, :].rearrange("p b s -> p (b s)")[:, 0:M],
                                            vecT[:, b0:b0 + SPG, 0:F], start=True, stop=True)
                    if i + 1 in [first + n for first, n in pieces(t, g)]:
                        last.then_inc(gram_done, 1)

            def layer1_dense(t):
                if t > 0:
                    pe.wait_ge(h2_set, N2 * t)
                    pe.wait_ge(y_set, t)
                else:
                    pe.wait_ge(wsum_set, 1)
                    pe.wait_ge(vec_set, 1)
                for n in range(N1):
                    nc.tensor.matmul(h1_psum(n // 2)[:, n % 2], w1_sum[:, n * P:(n + 1) * P],
                                     vecT[:, t * P:(t + 1) * P, DENSE], start=n % 2 == 0, stop=False,
                                     skip_group_check=True)

            def layer1_pairs(t, half):
                if t == 0:
                    pe.wait_ge(gaps_in, 16 * GAP_LOADS)
                    pe.wait_ge(w1_in, 16 * W1_LOADS)
                pe.wait_ge(pairs_act, NG * (t + 1))
                pe.wait_ge(pairs_dve, NG * (t + 1))
                for n in (2 * half, 2 * half + 1):
                    for c in range(NC):
                        last = nc.tensor.matmul(h1_psum(half)[:, n % 2], w1_pair[:, c, n * P:(n + 1) * P],
                                                pairs[:, c, t * P:(t + 1) * P], start=False, stop=c == NC - 1,
                                                skip_group_check=True)
                last.then_inc(mlp1_done, 1)

            def layer2(t, parts):
                if t == 0:
                    pe.wait_ge(w23_in, 48)
                pe.wait_ge(h1_act, t + 1)
                for half in range(2):
                    if half == 1:
                        pe.wait_ge(h1_dve, t + 1)
                    for n in parts:
                        for k in (2 * half, 2 * half + 1):
                            last = nc.tensor.matmul(h2_psum(t, n), w2[:, k, n * P:(n + 1) * P],
                                                    h1T[:, k, t * P:(t + 1) * P],
                                                    start=k == 0, stop=k == N1 - 1)
                        if half == 1 and t == NT - 1:
                            last.then_inc(mlp2_done, 1)
                if t < NT - 1 and N2 - 1 in parts:
                    last.then_inc(mlp2_done, N2)

            def layer3(t):
                for k in range(N2):
                    pe.wait_ge(h2_set, N2 * t + k + 1)
                    last = nc.tensor.matmul(y_psum, w3[:, k:k + 1], h2T[:, k, t * P:(t + 1) * P],
                                            start=k == 0, stop=k == N2 - 1)
                last.then_inc(mlp3_done, 1)

            pe.wait_ge(ident_set, 1)
            for _ in range(WARM):
                nc.tensor.matmul(mlp[1][:, 0], ident[:], ident[:], start=True, stop=True)
            for k in range(NF):
                look_up(k)
                for q in AFTER[k]:
                    transposes(0, q)
            layer1_dense(0)
            for t in range(1, NT):
                grams(t - 1, 0)
                transposes(t, 0)
                if t > 1:
                    layer3(t - 2)
                grams(t - 1, 1)
                grams(t - 1, 2)
                transposes(t, 1)
                grams(t - 1, 3)
                if t > 1:
                    layer1_dense(t - 1)
                else:
                    for k in range(NF, NH):
                        look_up(k)
                transposes(t, 2)
                layer1_pairs(t - 1, 0)
                transposes(t, 3)
                layer1_pairs(t - 1, 1)
                for q in range(4, NQ - 2):
                    transposes(t, q)
                if t < NT - 1:
                    transposes(t, NQ - 2)
                    layer2(t - 1, (0,))
                    transposes(t, NQ - 1)
                    layer2(t - 1, (1,))
                else:
                    layer2(t - 1, (0,))
                    transposes(t, NQ - 2)
                    layer2(t - 1, (1,))
                    transposes(t, NQ - 1)
            for g in range(NG):
                grams(NT - 1, g)
                if g == 0:
                    layer3(NT - 2)
            layer1_dense(NT - 1)
            layer1_pairs(NT - 1, 0)
            layer1_pairs(NT - 1, 1)
            layer2(NT - 1, (0, 1))
            layer3(NT - 1)


def kernel(**inputs):
    import numpy as np
    import concourse.bacc as bacc
    from concourse import mybir
    from concourse.bass_utils import run_bass_kernel_spmd

    nc = bacc.Bacc("TRN2", target_bir_lowering=False, num_devices=1)
    arrays, aps = {}, {}
    for name, value in inputs.items():
        a = np.ascontiguousarray(value)
        arrays[f"in_{name}"] = a
        aps[name] = nc.dram_tensor(f"in_{name}", a.shape, mybir.dt.from_np(a.dtype), kind="ExternalInput").ap()
    batch, features = inputs["ids"].shape
    cols = np.ascontiguousarray(np.asarray(inputs["ids"]).reshape(128, batch // 128, features)
                                .transpose(2, 1, 0).reshape(features, batch))
    arrays["in_ids_cols"] = cols
    ids_cols = nc.dram_tensor("in_ids_cols", cols.shape, mybir.dt.from_np(cols.dtype), kind="ExternalInput").ap()
    out = nc.dram_tensor("out_y", (batch, 1), mybir.dt.float32, kind="ExternalOutput").ap()
    dlrm_tower(nc, aps["r_dense_features"], aps["ids"], ids_cols, [aps[f"tbl_{f}"] for f in range(features)],
               aps["W_top1"], aps["b_top1"], aps["W_top2"], aps["b_top2"], aps["W_top3"], out)
    return run_bass_kernel_spmd(nc, [arrays], core_ids=[0]).results[0]["out_y"]
```
